# Optimizing a Trainium2 kernel written in Bass

```python
import numpy as np
import jax
import jax.numpy as jnp

def _softmax(x, axis=-1):
    return jax.nn.softmax(x, axis=axis)

def _gelu(x):
    return jax.nn.gelu(x, approximate=True)

def _silu(x):
    return jax.nn.silu(x)

def _sigmoid(x):
    return jax.nn.sigmoid(x)

def _layernorm(x, axis=-1, eps=1e-05):
    m = jnp.mean(x, axis=axis, keepdims=True)
    v = jnp.var(x, axis=axis, keepdims=True)
    return (x - m) / jnp.sqrt(v + eps)

def _scatter_add(tgt, idx, src, axis=0):
    return tgt.at[idx].add(src)

def _segment_sum(src, seg, n):
    return jax.ops.segment_sum(src, seg, n)
kernel_name = 'mk_adj_ffn_d1_adj_r2_1a12fd'

def setup_inputs(seed: int=0):
    np.random.seed(seed)
    _w = jnp.asarray

    def _rec_inputs():
        import jax
        import jax.numpy as jnp
        _gk = jax.random.key(seed)
        x = -0.0002928 + 1 * jax.random.normal(jax.random.fold_in(_gk, 1), (1354, 256), jnp.float32)
        _a = jax.random.bernoulli(jax.random.fold_in(_gk, 2), 0.0014771, (1354, 1354))
        adj = _a.astype(jnp.int32)
        return (x, adj)
    x, adj = _rec_inputs()

    def _L0_gnn_setup():
        import jax, jax.numpy as jnp
        import numpy as np
        N, D_IN, D_OUT = (4096, 256, 256)
        key = jax.random.key(seed)
        ks = jax.random.split(key, 8)
        scale_in = 1.0 / np.sqrt(D_IN)
        scale_cat = 1.0 / np.sqrt(2 * D_OUT)
        return {'x': jax.random.normal(ks[0], (N, D_IN), dtype=jnp.float32), 'adj': jax.random.randint(ks[1], (N, N), 0, 2, dtype=jnp.int32), 'W_self': jax.random.uniform(ks[2], (D_IN, D_OUT), jnp.float32, -scale_in, scale_in), 'b_self': jax.random.uniform(ks[3], (D_OUT,), jnp.float32, -scale_in, scale_in), 'W_nb': jax.random.uniform(ks[4], (D_IN, D_OUT), jnp.float32, -scale_in, scale_in), 'b_nb': jax.random.uniform(ks[5], (D_OUT,), jnp.float32, -scale_in, scale_in), 'W_comb': jax.random.uniform(ks[6], (2 * D_OUT, D_OUT), jnp.float32, -scale_cat, scale_cat), 'b_comb': jax.random.uniform(ks[7], (D_OUT,), jnp.float32, -scale_cat, scale_cat)}
    _L0_gnn_all = _L0_gnn_setup()
    _L0_gnn_in = {k: v for k, v in _L0_gnn_all.items() if k in ('W_self', 'b_self', 'W_nb', 'b_nb', 'W_comb', 'b_comb')}
    del _L0_gnn_all

    def _L0_ffn_setup():
        import jax, jax.numpy as jnp
        import numpy as np
        B, T, D = (4, 256, 256)
        N = 128
        key = jax.random.key(seed)
        ks = jax.random.split(key, 6)
        x = jax.random.normal(ks[0], (B, T, D), dtype=jnp.float32)
        positions = jax.random.normal(ks[1], (N, D), dtype=jnp.float32) * 0.1
        scales = jnp.ones((N,), dtype=jnp.float32) * 10.0
        value_weight = jax.random.normal(ks[2], (N, D, D), dtype=jnp.float32) * 0.02
        out_W = jax.random.normal(ks[3], (D, D), dtype=jnp.float32) * (1.0 / np.sqrt(D))
        out_b = jax.random.normal(ks[4], (D,), dtype=jnp.float32) * 0.01
        return {'x': x, 'positions': positions, 'scales': scales, 'value_weight': value_weight, 'out_W': out_W, 'out_b': out_b}
    _L0_ffn_all = _L0_ffn_setup()
    _L0_ffn_in = {k: v for k, v in _L0_ffn_all.items() if k in ('positions', 'scales', 'value_weight', 'out_W', 'out_b')}
    del _L0_ffn_all
    return {'x': x, 'adj': adj, 'L0_gnn_W_self': _L0_gnn_in['W_self'], 'L0_gnn_b_self': _L0_gnn_in['b_self'], 'L0_gnn_W_nb': _L0_gnn_in['W_nb'], 'L0_gnn_b_nb': _L0_gnn_in['b_nb'], 'L0_gnn_W_comb': _L0_gnn_in['W_comb'], 'L0_gnn_b_comb': _L0_gnn_in['b_comb'], 'L0_ffn_positions': _L0_ffn_in['positions'], 'L0_ffn_scales': _L0_ffn_in['scales'], 'L0_ffn_value_weight': _L0_ffn_in['value_weight'], 'L0_ffn_out_W': _L0_ffn_in['out_W'], 'L0_ffn_out_b': _L0_ffn_in['out_b']}

def reference(x, adj, L0_gnn_W_self, L0_gnn_b_self, L0_gnn_W_nb, L0_gnn_b_nb, L0_gnn_W_comb, L0_gnn_b_comb, L0_ffn_positions, L0_ffn_scales, L0_ffn_value_weight, L0_ffn_out_W, L0_ffn_out_b):
    import jax
    import jax.numpy as jnp

    def _L0_gnn_ref(x, adj, W_self, b_self, W_nb, b_nb, W_comb, b_comb):
        import jax, jax.numpy as jnp
        import numpy as np
        N, D_IN, D_OUT = (4096, 256, 256)
        mask = (adj > 0).astype(x.dtype)
        deg = jnp.sum(mask, axis=1, keepdims=True)
        agg = mask @ x / jnp.maximum(deg, 1.0)
        self_f = x @ W_self + b_self
        nb_f = agg @ W_nb + b_nb
        combined = jnp.concatenate([self_f, nb_f], axis=-1)
        out = combined @ W_comb + b_comb
        return jax.nn.relu(out)

    def _L0_ffn_ref(x, positions, scales, value_weight, out_W, out_b):
        import jax, jax.numpy as jnp
        import numpy as np
        B, T, D = (4, 256, 256)
        N = 128
        diff = x[:, :, None, :] - positions[None, None, :, :]
        distances = jnp.linalg.norm(diff, axis=-1)
        interactions = scales / (distances + 0.1)
        attn = jax.nn.softmax(interactions, axis=-1)
        out = jnp.einsum('btn,btd,nde->bte', attn, x, value_weight)
        return out @ out_W.T + out_b
    x = x + _L0_gnn_ref(_layernorm(x, axis=-1), adj, L0_gnn_W_self, L0_gnn_b_self, L0_gnn_W_nb, L0_gnn_b_nb, L0_gnn_W_comb, L0_gnn_b_comb)
    x = x + _L0_ffn_ref(_layernorm(x, axis=-1)[None], L0_ffn_positions, L0_ffn_scales, L0_ffn_value_weight, L0_ffn_out_W, L0_ffn_out_b)[0]
    return x

_drawn_inputs = setup_inputs


def setup_inputs(seed=0):
    import zlib

    import numpy as np

    out = dict(_drawn_inputs(seed))
    spreads = {'L0_ffn_scales': (10.0, 0.6)}
    factors = {'L0_gnn_b_self': 6.244,
     'L0_gnn_b_nb': 5.286,
     'L0_gnn_b_comb': 3.179,
     'L0_ffn_positions': 8.0,
     'L0_ffn_out_b': 5.94}
    for name, (base, spread) in spreads.items():
        noise = np.random.default_rng([zlib.crc32(name.encode()), seed]).standard_normal(out[name].shape)
        drawn = base * np.exp(spread * noise) if base else spread * noise
        out[name] = jnp.asarray(drawn.astype(out[name].dtype))
    for name, factor in factors.items():
        out[name] = (out[name] * factor).astype(out[name].dtype)
    return out
```

```python
from contextlib import ExitStack

import concourse.bass as bass
from concourse import mybir

F32 = mybir.dt.float32
F32R = mybir.dt.float32r
BF16 = mybir.dt.bfloat16
I32 = mybir.dt.int32
ALU = mybir.AluOpType
ACT = mybir.ActivationFunctionType
AX = mybir.AxisListType

P = 128
EPS = 1e-5
SOFTEN = 0.1
CHUNK = 4
UNROLL = 2
SLOTS = 4
ADJ_RING = 3


def gnn_ffn(nc, x, adj, W_self, b_self, W_nb, b_nb, W_comb, b_comb,
            positions, scales, value_weight, out_W, out_b, out):
    T, D = x.shape
    N = value_weight.shape[0]
    K = D // P
    TILES = -(-T // P)
    FULL = T // P
    TAIL = T - FULL * P
    LAST = TILES - 1
    CHUNKS = N // CHUNK
    TURNS = CHUNKS // UNROLL
    assert D == 2 * P and N == P and TAIL and CHUNKS % UNROLL == 0 and TILES > SLOTS

    def rows(t):
        return P if t < FULL else TAIL

    x_v = x[0:FULL * P, :].rearrange("(t p) d -> p t d", p=P)
    V_v = value_weight.rearrange("n (p k) e -> p n k e", k=K)

    ctx = ExitStack()
    with ctx:
        def sb(name, shape, dt=F32):
            return ctx.enter_context(nc.sbuf_tensor(name, shape, dt))

        def sem(name):
            return ctx.enter_context(nc.semaphore(name))

        x_sb = sb("x_sb", [P, TILES, D])
        normed = sb("normed", [P, TILES, D])
        skip = sb("skip", [P, TILES, D])
        acc = [skip, normed]
        xT_hi = sb("xT_hi", [P, K, T], F32R)
        xT_lo = sb("xT_lo", [P, K, T], F32R)
        y_hi = sb("y_hi", [P, TILES, D + 2], F32R)
        y_lo = sb("y_lo", [P, TILES, D], F32R)
        adj_sb = sb("adj_sb", [P, ADJ_RING, T], I32)
        mask = sb("mask", [P, 2, TILES * P], BF16)
        maskT = sb("maskT", [P, 2, TILES, P], F32R)
        attn = sb("attn", [P, TILES, N])
        attn_cur = sb("attn_cur", [P, UNROLL, TILES, CHUNK])
        v_raw = sb("v_raw", [P, UNROLL, CHUNK, K, D])
        v_hi = sb("v_hi", [P, UNROLL, CHUNK, K, D], F32R)
        v_lo = sb("v_lo", [P, UNROLL, CHUNK, K, D], F32R)

        w_self = sb("w_self", [P, K, D])
        w_nb = sb("w_nb", [P, K, D])
        w_comb = sb("w_comb", [P, 2, K, D])
        w_out = sb("w_out", [P, K, D])
        pos = sb("pos", [P, D])
        b_cols = sb("b_cols", [P, 2, K])
        b_comb_bc = sb("b_comb_bc", [P, D])
        b_out_bc = sb("b_out_bc", [P, D])
        scales_bc = sb("scales_bc", [P, N])
        wT = sb("wT", [P, 2, K, K, P])
        w12_hi = sb("w12_hi", [P, K, 2 * D], F32R)
        w12_lo = sb("w12_lo", [P, K, 2 * D], F32R)
        woT_hi = sb("woT_hi", [P, K, D], F32R)
        woT_lo = sb("woT_lo", [P, K, D], F32R)
        posT_hi = sb("posT_hi", [P, K, N], F32R)
        posT_lo = sb("posT_lo", [P, K, N], F32R)
        posT_sq = sb("posT_sq", [P, K, N])
        pos_norm = sb("pos_norm", [P, N])
        bias_bc = sb("bias_bc", [P, D])
        b_rep = sb("b_rep", [P, 2, K, P])
        ident = sb("ident", [P, P])
        ident16 = sb("ident16", [P, P], BF16)
        ones = sb("ones", [P, P])
        eps = sb("eps", [P, 1])
        stats = sb("stats", [P, TILES, 6])
        mv = sb("mv", [P, TILES, 2])
        std = sb("std", [P, TILES])
        rstd = sb("rstd", [P, TILES])
        shift = sb("shift", [P, TILES])
        z_norm = sb("z_norm", [P, TILES])
        rdeg = sb("rdeg", [P, TILES, 2])
        neg_max = sb("neg_max", [P, TILES])
        total = sb("total", [P, TILES])
        o_sum = sb("o_sum", [P, 2, D])
        oT_hi = sb("oT_hi", [P, 2, K, P], F32R)
        oT_lo = sb("oT_lo", [P, 2, K, P], F32R)
        result = b_rep[:].rearrange("p a k c -> p a (k c)")

        bank = [ctx.enter_context(nc.psum_tensor(f"bank{i}", [P, 512], F32)) for i in range(8)]

        weights_in = sem("weights_in")
        x_in = sem("x_in")
        adj_in = [sem(f"adj_in{r}") for r in range(ADJ_RING)]
        v_in = [sem(f"v_in{b}") for b in range(UNROLL)]
        consts_made = sem("consts_made")
        consts_step = sem("consts_step")
        bias_spread = sem("bias_spread")
        weights_turned = sem("weights_turned")
        weights_act = sem("weights_act")
        weights_dve = sem("weights_dve")
        weights_mult = sem("weights_mult")
        dve_step = sem("dve_step")
        moments1 = sem("moments1")
        std1 = sem("std1")
        scale1 = sem("scale1")
        norm1 = sem("norm1")
        turned1 = sem("turned1")
        xT1_hi = sem("xT1_hi")
        xT1_lo = sem("xT1_lo")
        proj = sem("proj")
        y_hi_made = sem("y_hi_made")
        y_made = sem("y_made")
        mask_made = sem("mask_made")
        mask_turned = sem("mask_turned")
        maskT_made = sem("maskT_made")
        agg = sem("agg")
        moments2 = sem("moments2")
        std2 = sem("std2")
        scale2 = sem("scale2")
        norm2 = sem("norm2")
        turned2 = sem("turned2")
        xT2_hi = sem("xT2_hi")
        xT2_lo = sem("xT2_lo")
        cross = sem("cross")
        dist2 = sem("dist2")
        dist = sem("dist")
        inter = sem("inter")
        exped = sem("exped")
        attn_made = sem("attn_made")
        acc_cleared = sem("acc_cleared")
        v_hi_made = sem("v_hi_made")
        v_made = sem("v_made")
        attn_cur_made = sem("attn_cur_made")
        products = sem("products")
        slot_free = sem("slot_free")
        half_added = sem("half_added")
        o_summed = sem("o_summed")
        o_turned = sem("o_turned")
        oT_hi_made = sem("oT_hi_made")
        oT_made = sem("oT_made")
        o_mult = sem("o_mult")
        result_made = sem("result_made")
        stored = [sem("stored0"), sem("stored1")]

        block = ctx.enter_context(nc.Block())

        def tok(t):
            return slice(t * P, t * P + rows(t))

        def three_passes(psum, stat_hi, stat_lo, mov_hi, mov_lo):
            for k in range(K):
                nc.tensor.matmul(psum, stat_hi(k), mov_hi(k), start=(k == 0), stop=False)
                nc.tensor.matmul(psum, stat_hi(k), mov_lo(k), start=False, stop=False)
                last = nc.tensor.matmul(psum, stat_lo(k), mov_hi(k), start=False, stop=(k == K - 1))
            return last

        turn_bank = [bank[6], bank[7]]
        prod_bank = [bank[4], bank[5]]
        mask_banks = [(bank[0], bank[1]), (bank[2], bank[3])]

        def slot_plan(last_turn):
            slots = [v % SLOTS for v in range(UNROLL * TILES)]
            if last_turn:
                first = (UNROLL - 1) * TILES
                slots[first:] = [v % (SLOTS - 1) for v in range(TILES)]
            used = {}
            for v in range(UNROLL * TILES):
                used[v % SLOTS] = v - UNROLL * TILES
            before = []
            for v, s in enumerate(slots):
                before.append(used[s])
                used[s] = v
            return slots, before

        LAST_TURN = TURNS - 1
        TURN_TILES = UNROLL * TILES

        @block.sync
        def _(sp):
            sp.dma_start(x_sb[:, 0:FULL, :], x_v).then_inc(x_in, 16)
            sp.dma_start(x_sb[0:TAIL, FULL, :], x[FULL * P:T, :]).then_inc(x_in, 16)
            for i in range(TILES):
                if i >= ADJ_RING:
                    sp.wait_ge(mask_made, i - ADJ_RING + 1)
                sp.dma_start(adj_sb[0:rows(i), i % ADJ_RING, :], adj[tok(i), :]).then_inc(adj_in[i % ADJ_RING], 16)
                if i == 3 or i == 5:
                    b = (i - 3) // 2
                    sp.dma_start(v_raw[:, b], V_v[:, b * CHUNK:(b + 1) * CHUNK]).then_inc(v_in[b], 16)
            for b in range(UNROLL):
                sp.wait_ge(v_made, b + 1)
                c = UNROLL + b
                sp.dma_start(v_raw[:, b], V_v[:, c * CHUNK:(c + 1) * CHUNK]).then_inc(v_in[b], 16)
            with nc.Fori(0, TURNS - 2, engines=[mybir.EngineType.SP]) as i:
                for b in range(UNROLL):
                    sp.wait_ge(v_made, i * UNROLL + (UNROLL + b + 1))
                    sp.dma_start(v_raw[:, b], V_v[:, bass.ds(i * (UNROLL * CHUNK) + (2 * UNROLL + b) * CHUNK, CHUNK)])\
                      .then_inc(v_in[b], 16)
            for t in range(TILES):
                sp.wait_ge(result_made, t + 1)
                sp.dma_start(out[tok(t), :], result[0:rows(t), t % 2]).then_inc(stored[t % 2], 16)
            sp.wait_ge(stored[0], 16 * ((TILES + 1) // 2))
            sp.wait_ge(stored[1], 16 * (TILES // 2))

        @block.gpsimd
        def _(pool):
            nc.gpsimd.memset(ident[:], 0.0).then_inc(consts_step, 1)
            nc.gpsimd.memset(ident16[:], 0.0).then_inc(consts_step, 1)
            nc.gpsimd.memset(ones[:], 1.0).then_inc(consts_made, 1)
            nc.gpsimd.memset(eps[:], EPS).then_inc(consts_made, 1)
            nc.gpsimd.memset(mv[:], 0.0).then_inc(consts_made, 1)
            nc.gpsimd.memset(mask[:, :, T:], 0.0).then_inc(consts_made, 1)
            nc.gpsimd.memset(attn[:, LAST, :], 0.0).then_inc(consts_made, 1)
            nc.gpsimd.memset(y_hi[:, :, D:D + 1].bitcast(F32), 1.0).then_inc(consts_made, 1)
            nc.gpsimd.memset(y_hi[:, :, D + 1:D + 2].bitcast(F32), 0.0).then_inc(consts_made, 1)
            for n, m in enumerate((ident, ident16)):
                pool.wait_ge(consts_step, n + 1)
                nc.gpsimd.affine_select(out=m[:], in_=m[:], compare_op=ALU.not_equal, fill=1.0, base=0,
                                        pattern=[[-1, P]], channel_multiplier=1).then_inc(consts_made, 1)
            pool.wait_ge(weights_in, 16 * 11)
            pool.wait_ge(consts_made, 1)
            for w in range(2):
                for k in range(K):
                    nc.gpsimd.tensor_scalar(b_rep[:, w, k], ones[:], b_cols[:, w, k:k + 1], None, ALU.mult)\
                      .then_inc(bias_spread, 1)
            for b in range(UNROLL):
                pool.wait_ge(v_hi_made, b + 1)
                nc.gpsimd.tensor_tensor(v_lo[:, b], v_raw[:, b], v_hi[:, b].bitcast(F32), ALU.subtract)\
                  .then_inc(v_made, 1)
            for t in range(TILES):
                r = rows(t)
                pool.wait_ge(norm2, t + 1)
                nc.gpsimd.tensor_tensor(x_sb[0:r, t], x_sb[0:r, t], b_out_bc[0:r, :], ALU.add)\
                  .then_inc(acc_cleared, 1)
                nc.gpsimd.memset(skip[:, t, :], 0.0).then_inc(acc_cleared, 1)
                pool.wait_ge(turned2, t + 1)
                nc.gpsimd.memset(normed[:, t, :], 0.0).then_inc(acc_cleared, 1)
            with nc.Fori(0, TURNS - 1, engines=[mybir.EngineType.Pool]) as i:
                for b in range(UNROLL):
                    pool.wait_ge(v_hi_made, i * UNROLL + (UNROLL + b + 1))
                    nc.gpsimd.tensor_tensor(v_lo[:, b], v_raw[:, b], v_hi[:, b].bitcast(F32), ALU.subtract)\
                      .then_inc(v_made, 1)

        @block.scalar
        def _(act):
            for dst, src in ((w_self[:], W_self.rearrange("(p k) o -> p k o", k=K)),
                             (w_nb[:], W_nb.rearrange("(p k) o -> p k o", k=K)),
                             (w_comb[:, 0], W_comb[0:D, :].rearrange("(p k) o -> p k o", k=K)),
                             (w_comb[:, 1], W_comb[D:2 * D, :].rearrange("(p k) o -> p k o", k=K)),
                             (pos[:], positions),
                             (w_out[:], out_W.rearrange("(b p) d -> p b d", p=P)),
                             (b_cols[:, 0], b_self.rearrange("(p k) -> p k", k=K)),
                             (b_cols[:, 1], b_nb.rearrange("(p k) -> p k", k=K)),
                             (b_comb_bc[:], b_comb.partition_broadcast(P)),
                             (b_out_bc[:], out_b.partition_broadcast(P)),
                             (scales_bc[:], scales.partition_broadcast(P))):
                act.dma_start(dst, src).then_inc(weights_in, 16)

            act.wait_ge(weights_turned, 1)
            nc.scalar.activation(wT[:, 0], bank[0][:].rearrange("p (o k d) -> p o k d", o=K, k=K), ACT.Copy)\
              .then_inc(weights_act, 1)
            act.wait_ge(weights_turned, 3)
            nc.scalar.activation(woT_hi[:], bank[2][:].rearrange("p (k n) -> p k n", k=K), ACT.Copy)\
              .then_inc(weights_act, 1)
            act.wait_ge(weights_turned, 4)
            pos_ps = bank[3][:, 0:K * N].rearrange("p (k n) -> p k n", k=K)
            nc.scalar.activation(posT_sq[:], pos_ps, ACT.Square).then_inc(weights_act, 1)
            nc.scalar.activation(posT_hi[:], pos_ps, ACT.Copy, scale=-2.0).then_inc(weights_act, 1)

            act.wait_ge(moments1, TILES)
            act.wait_ge(consts_made, 9)
            nc.scalar.activation(std[:], mv[:, :, 1], ACT.Sqrt, bias=eps[:]).then_inc(std1, 1)

            for w in range(2):
                act.wait_ge(weights_mult, w + 1)
                nc.scalar.activation(w12_hi[:, :, w * D:(w + 1) * D],
                                     bank[4 + w][:].rearrange("p (k n) -> p k n", k=K), ACT.Copy)\
                  .then_inc(weights_act, 1)

            def normalise(t, signal):
                r = rows(t)
                nc.scalar.activation(normed[0:r, t], x_sb[0:r, t], ACT.Identity, scale=rstd[0:r, t:t + 1],
                                     bias=shift[0:r, t:t + 1]).then_inc(signal, 1)

            def high_turned(t, signal):
                r = rows(t)
                src = turn_bank[t % 2][:, 0:K * P].rearrange("p (k c) -> p k c", k=K)[:, :, 0:r]
                nc.scalar.activation(xT_hi[:, :, tok(t)], src, ACT.Copy).then_inc(signal, 1)

            def evacuate_mask(i):
                act.wait_ge(mask_turned, i + 1)
                if i >= 2:
                    act.wait_ge(agg, i - 1)
                r = rows(i)
                lo, hi = mask_banks[i % 2]
                for b, first, count in ((lo, 0, 8), (hi, 8, TILES - 8)):
                    src = b[:].bitcast(BF16).rearrange("p (j c) -> p j c", c=P)[:, 0:count, 0:r]
                    nc.scalar.activation(maskT[:, i % 2, first:first + count, 0:r], src, ACT.Copy)\
                      .then_inc(maskT_made, 1)

            act.wait_ge(scale1, 1)
            normalise(0, norm1)
            normalise(1, norm1)
            for t in range(TILES + 1):
                if t < TILES:
                    act.wait_ge(turned1, t + 1)
                    high_turned(t, xT1_hi)
                if t + 2 < TILES:
                    normalise(t + 2, norm1)
                if t >= 1:
                    act.wait_ge(proj, t)
                    r = rows(t - 1)
                    nc.scalar.activation(y_hi[0:r, t - 1, 0:D], prod_bank[(t - 1) % 2][0:r, D:2 * D], ACT.Copy)\
                      .then_inc(y_hi_made, 1)
                if t in (5, 8):
                    evacuate_mask((t - 5) // 3)

            for s in range(TILES + 5):
                if s + 2 < TILES:
                    evacuate_mask(s + 2)
                if 0 <= s - 1 < TILES:
                    act.wait_ge(scale2, s)
                    normalise(s - 1, norm2)
                if 0 <= s - 2 < TILES:
                    act.wait_ge(turned2, s - 1)
                    high_turned(s - 2, xT2_hi)
                if s < TILES:
                    act.wait_ge(moments2, s + 1)
                    r = rows(s)
                    nc.scalar.activation(std[0:r, s:s + 1], mv[0:r, s, 1:2], ACT.Sqrt, bias=eps[0:r]).then_inc(std2, 1)
                if 0 <= s - 4 < TILES:
                    t = s - 4
                    r = rows(t)
                    act.wait_ge(dist2, t + 1)
                    nc.scalar.activation(attn[0:r, t], attn[0:r, t], ACT.Sqrt).then_inc(dist, 1)
                if s in (9, 10):
                    b = s - 9
                    act.wait_ge(v_in[b], 16)
                    nc.scalar.activation(v_hi[:, b], v_raw[:, b], ACT.Copy).then_inc(v_hi_made, 1)

            for t in range(TILES):
                r = rows(t)
                act.wait_ge(inter, t + 1)
                nc.scalar.activation(attn[0:r, t], attn[0:r, t], ACT.Exp, bias=neg_max[0:r, t:t + 1],
                                     accum_out=total[0:r, t:t + 1]).then_inc(exped, 1)
            act.wait_ge(attn_made, TILES)
            for b in range(UNROLL):
                nc.scalar.activation(attn_cur[:, b], attn[:, :, b * CHUNK:(b + 1) * CHUNK], ACT.Copy)\
                  .then_inc(attn_cur_made, 1)

            with nc.Fori(0, TURNS - 1, engines=[mybir.EngineType.Activation]) as i:
                for b in range(UNROLL):
                    act.wait_ge(v_in[b], i * 16 + 32)
                    act.wait_ge(products, i * TURN_TILES + (b + 1) * TILES)
                    nc.scalar.activation(v_hi[:, b], v_raw[:, b], ACT.Copy).then_inc(v_hi_made, 1)
                    act.wait_ge(slot_free, i * TURN_TILES + (b + 1) * TILES + SLOTS)
                    nc.scalar.activation(attn_cur[:, b],
                                         attn[:, :, bass.ds(i * (UNROLL * CHUNK) + (UNROLL + b) * CHUNK, CHUNK)],
                                         ACT.Copy).then_inc(attn_cur_made, 1)

            for t in range(TILES):
                r = rows(t)
                act.wait_ge(o_turned, t + 1)
                if t >= 2:
                    act.wait_ge(o_mult, t - 1)
                src = bank[6][:, 0:K * P].rearrange("p (k c) -> p k c", k=K)[:, :, 0:r]
                nc.scalar.activation(oT_hi[:, t % 2, :, 0:r], src, ACT.Copy).then_inc(oT_hi_made, 1)

        @block.vector
        def _(dve):
            steps = [0]

            def then(ins):
                steps[0] += 1
                ins.then_inc(dve_step, 1)
                dve.wait_ge(dve_step, steps[0])

            dve.wait_ge(x_in, 32)
            for t in range(TILES):
                r = rows(t)
                last = nc.vector.bn_stats(stats[0:r, t], x_sb[0:r, t])
            then(last)
            dve.wait_ge(consts_made, 9)
            for t in range(TILES):
                r = rows(t)
                nc.vector.bn_aggr(mv[0:r, t], stats[0:r, t]).then_inc(moments1, 1)

            dve.wait_ge(weights_turned, 2)
            nc.vector.tensor_copy(wT[:, 1], bank[1][:].rearrange("p (o k d) -> p o k d", o=K, k=K))\
              .then_inc(weights_dve, 1)
            dve.wait_ge(std1, 1)
            then(nc.vector.reciprocal(rstd[:], std[:]))
            nc.vector.scalar_tensor_tensor(shift[:], mv[:, :, 0], -1.0, rstd[:], ALU.mult, ALU.mult)\
              .then_inc(scale1, 1)
            dve.wait_ge(weights_act, 2)
            nc.vector.tensor_tensor(woT_lo[:], bank[2][:].rearrange("p (k n) -> p k n", k=K),
                                    woT_hi[:].bitcast(F32), ALU.subtract).then_inc(weights_dve, 1)
            dve.wait_ge(weights_act, 4)
            nc.vector.scalar_tensor_tensor(posT_lo[:], bank[3][:, 0:K * N].rearrange("p (k n) -> p k n", k=K), -2.0,
                                           posT_hi[:].bitcast(F32), ALU.mult, ALU.subtract).then_inc(weights_dve, 1)
            for w in range(2):
                dve.wait_ge(weights_act, 5 + w)
                nc.vector.tensor_tensor(w12_lo[:, :, w * D:(w + 1) * D],
                                        bank[4 + w][:].rearrange("p (k n) -> p k n", k=K),
                                        w12_hi[:, :, w * D:(w + 1) * D].bitcast(F32), ALU.subtract)\
                  .then_inc(weights_dve, 1)
            dve.wait_ge(weights_mult, 4)
            nc.vector.tensor_tensor(bias_bc[:], bank[6][:, 0:D], b_comb_bc[:], ALU.add).then_inc(weights_dve, 1)
            nc.vector.tensor_copy(pos_norm[:], bank[7][:, 0:N]).then_inc(weights_dve, 1)

            def low_turned(t, signal):
                r = rows(t)
                src = turn_bank[t % 2][:, 0:K * P].rearrange("p (k c) -> p k c", k=K)[:, :, 0:r]
                nc.vector.tensor_tensor(xT_lo[:, :, tok(t)], src, xT_hi[:, :, tok(t)].bitcast(F32), ALU.subtract)\
                  .then_inc(signal, 1)

            def make_mask(i):
                dve.wait_ge(adj_in[i % ADJ_RING], 16 * (i // ADJ_RING + 1))
                if i >= 2:
                    dve.wait_ge(mask_turned, i - 1)
                r = rows(i)
                nc.vector.tensor_scalar(mask[0:r, i % 2, 0:T], adj_sb[0:r, i % ADJ_RING, :], 0.0, None, ALU.is_gt)\
                  .then_inc(mask_made, 1)

            dve.wait_ge(weights_dve, 6)
            for t in range(TILES + 1):
                if t < TILES:
                    dve.wait_ge(xT1_hi, t + 1)
                    low_turned(t, xT1_lo)
                if t in (2, 5):
                    make_mask((t - 2) // 3)
                if t >= 1:
                    u = t - 1
                    r = rows(u)
                    dve.wait_ge(y_hi_made, u + 1)
                    nc.vector.tensor_tensor(y_lo[0:r, u], prod_bank[u % 2][0:r, D:2 * D],
                                            y_hi[0:r, u, 0:D].bitcast(F32), ALU.subtract)
                    nc.vector.tensor_tensor(skip[0:r, u], prod_bank[u % 2][0:r, 0:D], bias_bc[0:r, :], ALU.add)\
                      .then_inc(y_made, 1)

            for s in range(TILES + 5):
                if s + 2 < TILES:
                    make_mask(s + 2)
                if s < TILES:
                    r = rows(s)
                    dve.wait_ge(agg, s + 1)
                    ps = prod_bank[s % 2]
                    then(nc.vector.tensor_scalar(rdeg[0:r, s, 0:1], ps[0:r, D:D + 1], 1.0, None, ALU.max))
                    then(nc.vector.reciprocal(rdeg[0:r, s, 1:2], rdeg[0:r, s, 0:1]))
                    then(nc.vector.scalar_tensor_tensor(skip[0:r, s], ps[0:r, 0:D], rdeg[0:r, s, 1:2],
                                                        skip[0:r, s], ALU.mult, ALU.add))
                    then(nc.vector.scalar_tensor_tensor(x_sb[0:r, s], skip[0:r, s], 0.0, x_sb[0:r, s],
                                                        ALU.max, ALU.add))
                    then(nc.vector.bn_stats(stats[0:r, s], x_sb[0:r, s]))
                    nc.vector.bn_aggr(mv[0:r, s], stats[0:r, s]).then_inc(moments2, 1)
                if 0 <= s - 1 < TILES:
                    t = s - 1
                    r = rows(t)
                    dve.wait_ge(std2, t + 1)
                    then(nc.vector.reciprocal(rstd[0:r, t:t + 1], std[0:r, t:t + 1]))
                    nc.vector.scalar_tensor_tensor(shift[0:r, t:t + 1], mv[0:r, t, 0:1], -1.0, rstd[0:r, t:t + 1],
                                                   ALU.mult, ALU.mult).then_inc(scale2, 1)
                    then(nc.vector.tensor_tensor(z_norm[0:r, t:t + 1], mv[0:r, t, 1:2], rstd[0:r, t:t + 1], ALU.mult))
                    then(nc.vector.scalar_tensor_tensor(z_norm[0:r, t:t + 1], z_norm[0:r, t:t + 1], float(D),
                                                        rstd[0:r, t:t + 1], ALU.mult, ALU.mult))
                if 0 <= s - 2 < TILES:
                    dve.wait_ge(xT2_hi, s - 1)
                    low_turned(s - 2, xT2_lo)
                if 0 <= s - 3 < TILES:
                    t = s - 3
                    r = rows(t)
                    dve.wait_ge(cross, t + 1)
                    then(nc.vector.scalar_tensor_tensor(attn[0:r, t], turn_bank[t % 2][0:r, 256:256 + N],
                                                        z_norm[0:r, t:t + 1], pos_norm[0:r, :], ALU.add, ALU.add))
                    nc.vector.tensor_scalar(attn[0:r, t], attn[0:r, t], 0.0, None, ALU.max).then_inc(dist2, 1)
                if 0 <= s - 5 < TILES or (s == TILES + 4):
                    for t in ([s - 5] if s < TILES + 4 else [LAST]):
                        if s == TILES + 4 and s - 5 != LAST:
                            continue
                        r = rows(t)
                        dve.wait_ge(dist, t + 1)
                        then(nc.vector.tensor_scalar(attn[0:r, t], attn[0:r, t], SOFTEN, None, ALU.add))
                        then(nc.vector.reciprocal(attn[0:r, t], attn[0:r, t]))
                        then(nc.vector.tensor_tensor(attn[0:r, t], attn[0:r, t], scales_bc[0:r, :], ALU.mult))
                        then(nc.vector.reduce_max(neg_max[0:r, t:t + 1], attn[0:r, t], AX.X))
                        nc.vector.tensor_scalar(neg_max[0:r, t:t + 1], neg_max[0:r, t:t + 1], -1.0, None, ALU.mult)\
                          .then_inc(inter, 1)

            for t in range(TILES):
                r = rows(t)
                dve.wait_ge(exped, t + 1)
                then(nc.vector.reciprocal(total[0:r, t:t + 1], total[0:r, t:t + 1]))
                nc.vector.tensor_scalar(attn[0:r, t], attn[0:r, t], total[0:r, t:t + 1], None, ALU.mult)\
                  .then_inc(attn_made, 1)
            dve.wait_ge(acc_cleared, 3 * TILES)

            def add_products(turn, v, slot):
                b, t = divmod(v, TILES)
                r = rows(t)
                g = turn * TURN_TILES + v
                dve.wait_ge(products, g + 1)
                for n in range(CHUNK):
                    if n >= 2:
                        dve.wait_ge(half_added, g * 2 + (n - 1))
                    ps = bank[2 * slot + n // 2][0:r, (n % 2) * D:(n % 2 + 1) * D]
                    a = acc[n % 2][0:r, t]
                    ins = nc.vector.scalar_tensor_tensor(a, ps, attn_cur[0:r, b, t, n:n + 1], a, ALU.mult, ALU.add)
                    if n < 2:
                        ins.then_inc(half_added, 1)
                ins.then_inc(slot_free, 1)

            for n in range(SLOTS):
                nc.vector.memset(total[:, n:n + 1], 0.0).then_inc(slot_free, 1)

            slots, _ = slot_plan(False)
            with nc.Fori(0, TURNS - 1, engines=[mybir.EngineType.DVE], hint_back_edge=True) as i:
                for v in range(TURN_TILES):
                    if v % TILES == 0:
                        dve.wait_ge(attn_cur_made, i * UNROLL + (v // TILES + 1))
                    add_products(i, v, slots[v])

            def sum_halves(t):
                r = rows(t)
                if t >= 2:
                    dve.wait_ge(o_turned, t - 1)
                dve.wait_ge(slot_free, SLOTS + LAST_TURN * TURN_TILES + (UNROLL - 1) * TILES + t + 1)
                nc.vector.tensor_tensor(o_sum[0:r, t % 2], acc[0][0:r, t], acc[1][0:r, t], ALU.add)\
                  .then_inc(o_summed, 1)

            def low_sums(t):
                r = rows(t)
                dve.wait_ge(oT_hi_made, t + 1)
                src = bank[6][:, 0:K * P].rearrange("p (k c) -> p k c", k=K)[:, :, 0:r]
                nc.vector.tensor_tensor(oT_lo[:, t % 2, :, 0:r], src, oT_hi[:, t % 2, :, 0:r].bitcast(F32),
                                        ALU.subtract).then_inc(oT_made, 1)

            def finish(t):
                r = rows(t)
                dve.wait_ge(o_mult, t + 1)
                if t >= 2:
                    dve.wait_ge(stored[t % 2], 16 * (t // 2))
                nc.vector.tensor_tensor(result[0:r, t % 2], bank[7][0:r, 0:D], x_sb[0:r, t], ALU.add)\
                  .then_inc(result_made, 1)

            slots, _ = slot_plan(True)
            for v in range(TURN_TILES):
                if v % TILES == 0:
                    dve.wait_ge(attn_cur_made, LAST_TURN * UNROLL + v // TILES + 1)
                add_products(LAST_TURN, v, slots[v])
                t = v - (UNROLL - 1) * TILES
                if t >= 0:
                    sum_halves(t)
                if t >= 1:
                    low_sums(t - 1)
                if t >= 2:
                    finish(t - 2)
            low_sums(LAST)
            finish(LAST - 1)
            finish(LAST)

        @block.tensor
        def _(pe):
            pe.wait_ge(consts_made, 9)
            pe.wait_ge(weights_in, 16 * 11)
            for w, src in enumerate((w_self, w_nb)):
                for ko in range(K):
                    for kd in range(K):
                        at = (ko * K + kd) * P
                        last = nc.tensor.transpose(bank[w][:, at:at + P], src[:, kd, ko::K], ident[:])
                last.then_inc(weights_turned, 1)
            for k in range(K):
                for b in range(K):
                    at = (k * K + b) * P
                    last = nc.tensor.transpose(bank[2][:, at:at + P], w_out[:, b, k::K], ident[:])
            last.then_inc(weights_turned, 1)
            for k in range(K):
                last = nc.tensor.transpose(bank[3][:, k * N:(k + 1) * N], pos[:, k::K], ident[:])
            last.then_inc(weights_turned, 1)
            for w in range(2):
                if w == 0:
                    pe.wait_ge(weights_act, 1)
                else:
                    pe.wait_ge(weights_dve, 1)
                for kd in range(K):
                    for ko in range(K):
                        last = nc.tensor.matmul(bank[4 + w][:, kd * D:(kd + 1) * D], wT[:, w, ko, kd],
                                                w_comb[:, w, ko], start=(ko == 0), stop=(ko == K - 1))
                last.then_inc(weights_mult, 1)
            pe.wait_ge(bias_spread, 2 * K)
            for w in range(2):
                for k in range(K):
                    last = nc.tensor.matmul(bank[6][:, 0:D], b_rep[:, w, k], w_comb[:, w, k],
                                            start=(w == k == 0), stop=(w == 1 and k == K - 1))
            last.then_inc(weights_mult, 1)
            pe.wait_ge(weights_act, 3)
            for k in range(K):
                last = nc.tensor.matmul(bank[7][:, 0:N], ones[:], posT_sq[:, k], start=(k == 0), stop=(k == K - 1))
            last.then_inc(weights_mult, 1)

            def turn_tokens(t, signal):
                r = rows(t)
                for k in range(K):
                    last = nc.tensor.transpose(turn_bank[t % 2][:, k * P:k * P + r], normed[0:r, t, k::K],
                                               ident[0:r, 0:r])
                last.then_inc(signal, 1)

            def turn_mask(i):
                r = rows(i)
                pe.wait_ge(mask_made, i + 1)
                if i >= 2:
                    pe.wait_ge(maskT_made, 2 * (i - 1))
                lo, hi = mask_banks[i % 2]
                for j in range(TILES):
                    dst = (lo if j < 8 else hi)[:].bitcast(BF16)
                    at = (j % 8) * P
                    last = nc.tensor.transpose(dst[:, at:at + r], mask[0:r, i % 2, j * P:(j + 1) * P],
                                               ident16[0:r, 0:r])
                last.then_inc(mask_turned, 1)

            pe.wait_ge(weights_dve, 7)
            for t in range(TILES + 1):
                if t < TILES:
                    pe.wait_ge(norm1, t + 1)
                    if t >= 2:
                        pe.wait_ge(xT1_lo, t - 1)
                    turn_tokens(t, turned1)
                if t >= 1:
                    u = t - 1
                    r = rows(u)
                    pe.wait_ge(xT1_lo, u + 1)
                    if u >= 2:
                        pe.wait_ge(y_made, u - 1)
                    three_passes(prod_bank[u % 2][0:r, :], lambda k: xT_hi[:, k, tok(u)], lambda k: xT_lo[:, k, tok(u)],
                                 lambda k: w12_hi[:, k], lambda k: w12_lo[:, k]).then_inc(proj, 1)
                if t in (4, 7):
                    turn_mask((t - 4) // 3)

            for s in range(TILES + 3):
                if s < TILES:
                    r = rows(s)
                    if s == 0:
                        pe.wait_ge(y_made, TILES)
                    pe.wait_ge(maskT_made, 2 * (s + 1))
                    if s >= 2:
                        pe.wait_ge(moments2, s - 1)
                    for j in range(TILES):
                        c = rows(j)
                        nc.tensor.matmul(prod_bank[s % 2][0:r, 0:D + 2], maskT[0:c, s % 2, j, 0:r], y_hi[0:c, j],
                                         start=(j == 0), stop=False)
                        last = nc.tensor.matmul(prod_bank[s % 2][0:r, 0:D], maskT[0:c, s % 2, j, 0:r], y_lo[0:c, j],
                                                start=False, stop=(j == LAST))
                    last.then_inc(agg, 1)
                if s + 2 < TILES:
                    turn_mask(s + 2)
                if 0 <= s - 2 < TILES:
                    t = s - 2
                    pe.wait_ge(norm2, t + 1)
                    if t >= 2:
                        pe.wait_ge(dist2, t - 1)
                    turn_tokens(t, turned2)
                if 0 <= s - 3 < TILES:
                    t = s - 3
                    r = rows(t)
                    pe.wait_ge(xT2_lo, t + 1)
                    three_passes(turn_bank[t % 2][0:r, 256:256 + N], lambda k: xT_hi[:, k, tok(t)],
                                 lambda k: xT_lo[:, k, tok(t)], lambda k: posT_hi[:, k], lambda k: posT_lo[:, k])\
                        .then_inc(cross, 1)
            pe.wait_ge(dist2, TILES)

            def multiply(turn, v, slot, before):
                b, t = divmod(v, TILES)
                r = rows(t)
                g = turn * TURN_TILES
                pe.wait_ge(slot_free, g + (before + 1 + SLOTS))
                pairs = [(bank[2 * slot + h][0:r, :], v_hi[:, b, 2 * h:2 * h + 2], v_lo[:, b, 2 * h:2 * h + 2])
                         for h in range(CHUNK // 2)]
                for k in range(K):
                    hi, lo = xT_hi[:, k, tok(t)], xT_lo[:, k, tok(t)]
                    for ps, vh, vl in pairs:
                        nc.tensor.matmul(ps, hi, vh[:, :, k], start=(k == 0), stop=False)
                    for ps, vh, vl in pairs:
                        nc.tensor.matmul(ps, hi, vl[:, :, k], start=False, stop=False)
                    for ps, vh, vl in pairs:
                        last = nc.tensor.matmul(ps, lo, vh[:, :, k], start=False, stop=(k == K - 1))
                last.then_inc(products, 1)

            slots, before = slot_plan(False)
            with nc.Fori(0, TURNS - 1, engines=[mybir.EngineType.PE], hint_back_edge=True) as i:
                for v in range(TURN_TILES):
                    if v % TILES == 0:
                        pe.wait_ge(v_made, i * UNROLL + (v // TILES + 1))
                    multiply(i, v, slots[v], before[v])

            def turn_sums(t):
                r = rows(t)
                pe.wait_ge(o_summed, t + 1)
                if t == 0:
                    last_use = max(v for v in range((UNROLL - 1) * TILES) if v % SLOTS == SLOTS - 1)
                    pe.wait_ge(slot_free, SLOTS + LAST_TURN * TURN_TILES + last_use + 1)
                else:
                    pe.wait_ge(oT_made, t)
                for k in range(K):
                    last = nc.tensor.transpose(bank[6][:, k * P:k * P + r], o_sum[0:r, t % 2, k::K], ident[0:r, 0:r])
                last.then_inc(o_turned, 1)

            def project_out(t):
                r = rows(t)
                pe.wait_ge(oT_made, t + 1)
                if t >= 1:
                    pe.wait_ge(result_made, t)
                three_passes(bank[7][0:r, 0:D], lambda k: oT_hi[:, t % 2, k, 0:r], lambda k: oT_lo[:, t % 2, k, 0:r],
                             lambda k: woT_hi[:, k], lambda k: woT_lo[:, k]).then_inc(o_mult, 1)

            slots, before = slot_plan(True)
            for v in range(TURN_TILES):
                if v % TILES == 0:
                    pe.wait_ge(v_made, LAST_TURN * UNROLL + v // TILES + 1)
                multiply(LAST_TURN, v, slots[v], before[v])
                t = v - (UNROLL - 1) * TILES
                if t >= 1:
                    turn_sums(t - 1)
                if t >= 2:
                    project_out(t - 2)
            turn_sums(LAST)
            project_out(LAST - 1)
            project_out(LAST)


_INS = ['x', 'adj', 'L0_gnn_W_self', 'L0_gnn_b_self', 'L0_gnn_W_nb', 'L0_gnn_b_nb', 'L0_gnn_W_comb', 'L0_gnn_b_comb',
        'L0_ffn_positions', 'L0_ffn_scales', 'L0_ffn_value_weight', 'L0_ffn_out_W', 'L0_ffn_out_b']


def kernel(**inputs):
    import numpy as _np
    import concourse.bacc as _bacc
    from concourse import mybir as _mybir
    from concourse.bass_utils import run_bass_kernel_spmd as _run

    nc = _bacc.Bacc("TRN2", target_bir_lowering=False, num_devices=1)
    arrays, args = {}, []
    for name in _INS:
        a = _np.ascontiguousarray(inputs[name])
        arrays[f"in_{name}_dram"] = a
        args.append(nc.dram_tensor(f"in_{name}_dram", a.shape, _mybir.dt.from_np(a.dtype), kind="ExternalInput").ap())
    shape = tuple(inputs['x'].shape)
    args.append(nc.dram_tensor("out_0_dram", shape, _mybir.dt.float32, kind="ExternalOutput").ap())
    gnn_ffn(nc, *args)
    r = _run(nc, [arrays], core_ids=[0])
    return r.results[0]["out_0_dram"]
```

```python
from contextlib import ExitStack

import concourse.bass as bass
from concourse import mybir

F32 = mybir.dt.float32
F32R = mybir.dt.float32r
BF16 = mybir.dt.bfloat16
I32 = mybir.dt.int32
ALU = mybir.AluOpType
ACT = mybir.ActivationFunctionType

P = 128
EPS = 1e-5
SOFTEN = 0.1
LOWEST = -3.0e38
CHUNK = 4
UNROLL = 2
SLOTS = 4
ADJ_RING = 3
POOL_MASKS = 5
WARMING = 4
REST_LOADS = 3
GROUP = 4
MASKS_MADE_AT = (6, 8, 12)
MASKS_AT = (8, 10)
SPLIT0_AT = 5


def gnn_ffn(nc, x, adj, W_self, b_self, W_nb, b_nb, W_comb, b_comb,
            positions, scales, value_weight, out_W, out_b, out):
    T, D = x.shape
    N = value_weight.shape[0]
    K = D // P
    TILES = -(-T // P)
    FULL = T // P
    TAIL = T - FULL * P
    LAST = TILES - 1
    CHUNKS = N // CHUNK
    TURNS = CHUNKS // UNROLL
    assert D == 2 * P and N == P and TAIL and CHUNKS % UNROLL == 0 and TILES > SLOTS

    def rows(t):
        return P if t < FULL else TAIL

    x_v = x[0:FULL * P, :].rearrange("(t p) d -> p t d", p=P)
    V_v = value_weight.rearrange("n (p k) e -> p n k e", k=K)

    ctx = ExitStack()
    with ctx:
        def sb(name, shape, dt=F32):
            return ctx.enter_context(nc.sbuf_tensor(name, shape, dt))

        def sem(name):
            return ctx.enter_context(nc.semaphore(name))

        x_sb = sb("x_sb", [P, TILES, D])
        normed = sb("normed", [P, TILES, D])
        skip = sb("skip", [P, TILES, D])
        acc = [skip, normed]
        xT_hi = sb("xT_hi", [P, K, T], F32R)
        xT_lo = sb("xT_lo", [P, K, T], F32R)
        y_hi = sb("y_hi", [P, TILES, D + 2], F32R)
        y_lo = sb("y_lo", [P, TILES, D], F32R)
        adj_sb = sb("adj_sb", [P, ADJ_RING, T], I32)
        mask = sb("mask", [P, 2, TILES * P], BF16)
        maskT = sb("maskT", [P, 2, TILES, P], F32R)
        attn = sb("attn", [P, TILES, N])
        attn_cur = sb("attn_cur", [P, UNROLL, TILES, CHUNK])
        v_raw = sb("v_raw", [P, UNROLL, CHUNK, K, D])
        v_hi = sb("v_hi", [P, UNROLL, CHUNK, K, D], F32R)
        v_lo = sb("v_lo", [P, UNROLL, CHUNK, K, D], F32R)

        w_self = sb("w_self", [P, K, D])
        w_nb = sb("w_nb", [P, K, D])
        w_comb = sb("w_comb", [P, 2, K, D])
        w_out = sb("w_out", [P, K, D])
        pos = sb("pos", [P, D])
        b_cols = sb("b_cols", [P, 2, K])
        b_comb_bc = sb("b_comb_bc", [P, D])
        b_out_bc = sb("b_out_bc", [P, D])
        scales_bc = sb("scales_bc", [P, N])
        wT = sb("wT", [P, 2, K, K, P])
        w12_hi = sb("w12_hi", [P, K, 2 * D], F32R)
        w12_lo = sb("w12_lo", [P, K, 2 * D], F32R)
        woT_hi = sb("woT_hi", [P, K, D], F32R)
        woT_lo = sb("woT_lo", [P, K, D], F32R)
        posT_hi = sb("posT_hi", [P, K, N], F32R)
        posT_lo = sb("posT_lo", [P, K, N], F32R)
        posT_sq = sb("posT_sq", [P, K, N])
        pos_norm = sb("pos_norm", [P, N])
        bias_bc = sb("bias_bc", [P, D])
        b_rep = sb("b_rep", [P, 2, K, P])
        ident = sb("ident", [P, P])
        ident16 = sb("ident16", [P, P], BF16)
        ones = sb("ones", [P, P])
        eps = sb("eps", [P, 1])
        stats = sb("stats", [P, TILES, 6])
        mv = sb("mv", [P, TILES, 2])
        std = sb("std", [P, TILES])
        rstd = sb("rstd", [P, TILES])
        shift = sb("shift", [P, TILES])
        z_norm = sb("z_norm", [P, TILES])
        rdeg = sb("rdeg", [P, TILES, 2])
        neg_max = sb("neg_max", [P, TILES])
        total = sb("total", [P, TILES])
        o_sum = sb("o_sum", [P, 2, D])
        oT_hi = sb("oT_hi", [P, 2, K, P], F32R)
        oT_lo = sb("oT_lo", [P, 2, K, P], F32R)
        result = [b_rep[:, t % 2].rearrange("p k c -> p (k c)") for t in range(TILES - 1)] + [o_sum[:, TILES % 2]]

        bank = [ctx.enter_context(nc.psum_tensor(f"bank{i}", [P, 512], F32)) for i in range(8)]

        w_self_in = sem("w_self_in")
        w_nb_in = sem("w_nb_in")
        w_comb_in = [sem("w_comb_in0"), sem("w_comb_in1")]
        pos_in = sem("pos_in")
        b_cols_in = sem("b_cols_in")
        b_comb_in = sem("b_comb_in")
        x_in = [sem(f"x_in{g}") for g in range(3)]
        rest_in = sem("rest_in")
        adj_in = [sem(f"adj_in{r}") for r in range(ADJ_RING)]
        v_in = [sem(f"v_in{b}") for b in range(UNROLL)]
        consts_made = sem("consts_made")
        consts_step = sem("consts_step")
        bias_spread = sem("bias_spread")
        weights_turned = sem("weights_turned")
        weights_act = sem("weights_act")
        weights_dve = sem("weights_dve")
        weights_mult = sem("weights_mult")
        dve_step = sem("dve_step")
        moments1 = sem("moments1")
        std1 = sem("std1")
        scale1 = sem("scale1")
        norm1 = sem("norm1")
        turned1 = sem("turned1")
        xT1_hi = sem("xT1_hi")
        xT1_lo = sem("xT1_lo")
        proj = sem("proj")
        y_hi_made = sem("y_hi_made")
        y_made = sem("y_made")
        mask_made = sem("mask_made")
        mask_turned = sem("mask_turned")
        maskT_made = sem("maskT_made")
        agg = sem("agg")
        agg_read = sem("agg_read")
        moments2 = sem("moments2")
        std2 = sem("std2")
        scale2 = sem("scale2")
        norm2 = sem("norm2")
        turned2 = sem("turned2")
        xT2_hi = sem("xT2_hi")
        xT2_lo = sem("xT2_lo")
        cross = sem("cross")
        dist2 = sem("dist2")
        dist = sem("dist")
        inter = sem("inter")
        exped = sem("exped")
        total_inv = sem("total_inv")
        attn_made = sem("attn_made")
        z_norm_made = sem("z_norm_made")
        residual_made = sem("residual_made")
        v_hi_made = sem("v_hi_made")
        v_made = sem("v_made")
        attn_cur_made = sem("attn_cur_made")
        products = sem("products")
        slot_free = sem("slot_free")
        half_added = sem("half_added")
        o_summed = sem("o_summed")
        o_turned = sem("o_turned")
        oT_hi_made = sem("oT_hi_made")
        oT_made = sem("oT_made")
        o_mult = sem("o_mult")
        result_made = sem("result_made")
        stored = [sem("stored0"), sem("stored1")]

        block = ctx.enter_context(nc.Block())

        def tok(t):
            return slice(t * P, t * P + rows(t))

        def three_passes(psum, stat_hi, stat_lo, mov_hi, mov_lo):
            for k in range(K):
                nc.tensor.matmul(psum, stat_hi(k), mov_hi(k), start=(k == 0), stop=False)
                nc.tensor.matmul(psum, stat_hi(k), mov_lo(k), start=False, stop=False)
                last = nc.tensor.matmul(psum, stat_lo(k), mov_hi(k), start=False, stop=(k == K - 1))
            return last

        wT_bank = [bank[0], bank[1]]
        w12_bank = [bank[4], bank[5]]
        bias_bank = bank[6]
        pos_bank, out_w_bank = bank[7], bank[7]
        mask_banks = (bank[0], bank[1])
        turn1_bank = [bank[2], bank[3]]
        proj_bank = [bank[4], bank[5], bank[6], bank[7]]
        turn2_bank = [bank[2]] * LAST + [bank[3]]
        agg_bank = bank[3]
        CROSS = K * P
        TURN_TILES = UNROLL * TILES
        LAST_TURN = TURNS - 1
        groups = [slice(0, GROUP), slice(GROUP, 2 * GROUP), slice(2 * GROUP, TILES)]

        LAG = [2, 4]
        STEPS = TILES + LAG[1]
        first_turn = [(s, b, s - LAG[b]) for s in range(STEPS) for b in (1, 0) if 0 <= s - LAG[b] < TILES]
        first_slots = [2 + n % 2 for n in range(TURN_TILES)]
        CHUNK0_DONE = 1 + max(n for n, (_, b, _) in enumerate(first_turn) if b == 0)

        SHORT = (SLOTS - 1) * (-TURN_TILES % SLOTS)
        LAST_CHUNK = TURN_TILES - TILES

        def slot_plan(last_turn):
            slots = [v % (SLOTS - 1) if v < SHORT else (v - SHORT) % SLOTS for v in range(TURN_TILES)]
            used = {slot: v - TURN_TILES for v, slot in enumerate(slots)}
            if last_turn:
                slots[LAST_CHUNK:] = [(slots[LAST_CHUNK - 1] + 1 + t) % (SLOTS - 1) for t in range(TILES)]
            before = []
            for v, slot in enumerate(slots):
                before.append(used[slot])
                used[slot] = v
            return slots, before

        last_slots, last_before = slot_plan(True)
        o_banks = [(bank[6], bank[7])] * LAST + [(bank[2 * last_slots[-3]], bank[2 * last_slots[-3] + 1])]

        halves = lambda ap, r: ap[:, 0:K * P].rearrange("p (k c) -> p k c", k=K)[:, :, 0:r]

        @block.sync
        def _(sp):
            for dst, src, signal in (
                    (w_self[:], W_self.rearrange("(p k) o -> p k o", k=K), w_self_in),
                    (w_nb[:], W_nb.rearrange("(p k) o -> p k o", k=K), w_nb_in),
                    (w_comb[:, 0], W_comb[0:D, :].rearrange("(p k) o -> p k o", k=K), w_comb_in[0]),
                    (w_comb[:, 1], W_comb[D:2 * D, :].rearrange("(p k) o -> p k o", k=K), w_comb_in[1]),
                    (b_cols[:, 0], b_self.rearrange("(p k) -> p k", k=K), b_cols_in),
                    (b_cols[:, 1], b_nb.rearrange("(p k) -> p k", k=K), b_cols_in),
                    (x_sb[:, groups[0]], x_v[:, groups[0]], x_in[0]),
                    (x_sb[:, groups[1]], x_v[:, groups[1]], x_in[1]),
                    (pos[:], positions, pos_in),
                    (b_comb_bc[:], b_comb.partition_broadcast(P), b_comb_in),
                    (x_sb[:, 2 * GROUP:FULL], x_v[:, 2 * GROUP:], x_in[2]),
                    (x_sb[0:TAIL, FULL, :], x[FULL * P:T, :], x_in[2])):
                sp.dma_start(dst, src).then_inc(signal, 16)
            for i in range(TILES):
                if i >= ADJ_RING:
                    sp.wait_ge(mask_made, i - ADJ_RING + 1)
                sp.dma_start(adj_sb[0:rows(i), i % ADJ_RING, :], adj[tok(i), :]).then_inc(adj_in[i % ADJ_RING], 16)
                if i < UNROLL:
                    sp.dma_start(v_raw[:, i], V_v[:, i * CHUNK:(i + 1) * CHUNK]).then_inc(v_in[i], 16)
                if i == 1:
                    sp.dma_start(w_out[:], out_W.rearrange("(b p) d -> p b d", p=P)).then_inc(rest_in, 16)
                    sp.dma_start(b_out_bc[:], out_b.partition_broadcast(P)).then_inc(rest_in, 16)
                    sp.dma_start(scales_bc[:], scales.partition_broadcast(P)).then_inc(rest_in, 16)
                if i == 4:
                    for b in range(UNROLL):
                        c = UNROLL + b
                        sp.wait_ge(v_made, b + 1)
                        sp.dma_start(v_raw[:, b], V_v[:, c * CHUNK:(c + 1) * CHUNK]).then_inc(v_in[b], 16)
            with nc.Fori(0, TURNS - 2, engines=[mybir.EngineType.SP]) as i:
                for b in range(UNROLL):
                    sp.wait_ge(v_made, i * UNROLL + (UNROLL + b + 1))
                    sp.dma_start(v_raw[:, b], V_v[:, bass.ds(i * (UNROLL * CHUNK) + (2 * UNROLL + b) * CHUNK, CHUNK)])\
                      .then_inc(v_in[b], 16)
            for t in range(TILES):
                sp.wait_ge(result_made, t + 1)
                sp.dma_start(out[tok(t), :], result[t][0:rows(t)]).then_inc(stored[t % 2], 16)
            sp.wait_ge(stored[0], 16 * ((TILES + 1) // 2))
            sp.wait_ge(stored[1], 16 * (TILES // 2))

        @block.gpsimd
        def _(pool):
            nc.gpsimd.memset(ident[:], 0.0).then_inc(consts_step, 1)
            nc.gpsimd.memset(ident16[:], 0.0).then_inc(consts_step, 1)
            nc.gpsimd.memset(ones[:], 1.0).then_inc(consts_made, 1)
            nc.gpsimd.memset(eps[:], EPS).then_inc(consts_made, 1)
            nc.gpsimd.memset(mv[:, LAST], 0.0).then_inc(consts_made, 1)
            for n, m in enumerate((ident, ident16)):
                pool.wait_ge(consts_step, n + 1)
                nc.gpsimd.affine_select(out=m[:], in_=m[:], compare_op=ALU.not_equal, fill=1.0, base=0,
                                        pattern=[[-1, P]], channel_multiplier=1).then_inc(consts_made, 1)
            nc.gpsimd.memset(mask[:, :, T:], 0.0).then_inc(consts_made, 1)
            nc.gpsimd.memset(attn[:, LAST, :], 0.0).then_inc(consts_made, 1)
            nc.gpsimd.memset(y_hi[:, :, D:D + 1].bitcast(F32), 1.0).then_inc(consts_made, 1)
            nc.gpsimd.memset(y_hi[:, :, D + 1:D + 2].bitcast(F32), 0.0).then_inc(consts_made, 1)
            for t in range(TILES):
                r = rows(t)
                pool.wait_ge(scale1, min(t // GROUP, 2) + 1)
                nc.gpsimd.tensor_scalar(normed[0:r, t], x_sb[0:r, t], rstd[0:r, t:t + 1], shift[0:r, t:t + 1],
                                        ALU.mult, ALU.add).then_inc(norm1, 1)
            for b in range(UNROLL):
                pool.wait_ge(v_hi_made, b + 1)
                nc.gpsimd.tensor_tensor(v_lo[:, b], v_raw[:, b], v_hi[:, b].bitcast(F32), ALU.subtract)\
                  .then_inc(v_made, 1)

            def make_mask(i):
                pool.wait_ge(adj_in[i % ADJ_RING], 16 * (i // ADJ_RING + 1))
                if i >= 2:
                    pool.wait_ge(mask_turned, i - 1)
                r = rows(i)
                nc.gpsimd.tensor_scalar(mask[0:r, i % 2, 0:T], adj_sb[0:r, i % ADJ_RING, :], 0.0, None, ALU.is_gt)\
                  .then_inc(mask_made, 1)

            pool.wait_ge(mask_made, POOL_MASKS)
            for t in range(TILES):
                r = rows(t)
                if POOL_MASKS <= t + 3 < TILES:
                    make_mask(t + 3)
                pool.wait_ge(scale2, t + 1)
                nc.gpsimd.tensor_scalar(z_norm[0:r, t:t + 1], mv[0:r, t, 1:2], rstd[0:r, t:t + 1], rstd[0:r, t:t + 1],
                                        ALU.mult, ALU.mult).then_inc(z_norm_made, 1)
                pool.wait_ge(norm2, t + 1)
                nc.gpsimd.tensor_tensor(x_sb[0:r, t], x_sb[0:r, t], b_out_bc[0:r, :], ALU.add)\
                  .then_inc(residual_made, 1)
            pool.wait_ge(v_hi_made, UNROLL + 2)
            pool.wait_ge(v_made, UNROLL + 1)
            nc.gpsimd.tensor_tensor(v_lo[:, 1], v_raw[:, 1], v_hi[:, 1].bitcast(F32), ALU.subtract).then_inc(v_made, 1)
            with nc.Fori(1, TURNS - 1, engines=[mybir.EngineType.Pool]) as i:
                for b in range(UNROLL):
                    pool.wait_ge(v_hi_made, i * UNROLL + (UNROLL + b + 1))
                    nc.gpsimd.tensor_tensor(v_lo[:, b], v_raw[:, b], v_hi[:, b].bitcast(F32), ALU.subtract)\
                      .then_inc(v_made, 1)

        @block.scalar
        def _(act):
            def deviations(g):
                act.wait_ge(moments1, groups[g].stop)
                nc.scalar.activation(std[:, groups[g]], mv[:, groups[g], 1], ACT.Sqrt, bias=eps[:]).then_inc(std1, 1)

            act.wait_ge(consts_made, 3)
            nc.scalar.activation(total[:, 0:1], eps[:], ACT.Sqrt)
            for w in range(2):
                act.wait_ge(weights_turned, w + 1)
                nc.scalar.activation(wT[:, w], wT_bank[w][:].rearrange("p (o k d) -> p o k d", o=K, k=K), ACT.Copy)\
                  .then_inc(weights_act, 1)
            deviations(0)
            for w in range(2):
                act.wait_ge(weights_mult, w + 1)
                nc.scalar.activation(w12_hi[:, :, w * D:(w + 1) * D],
                                     w12_bank[w][:].rearrange("p (k n) -> p k n", k=K), ACT.Copy)\
                  .then_inc(weights_act, 1)

            def high_tokens1(t):
                act.wait_ge(turned1, t + 1)
                nc.scalar.activation(xT_hi[:, :, tok(t)], halves(turn1_bank[t % 2], rows(t)), ACT.Copy)\
                  .then_inc(xT1_hi, 1)

            for t in range(2):
                high_tokens1(t)
            deviations(1)
            act.wait_ge(weights_turned, 3)
            pos_ps = pos_bank[:, 0:K * N].rearrange("p (k n) -> p k n", k=K)
            nc.scalar.activation(posT_sq[:], pos_ps, ACT.Square, scale=D ** -0.5).then_inc(weights_act, 1)
            nc.scalar.activation(posT_hi[:], pos_ps, ACT.Copy, scale=-2.0 / D).then_inc(weights_act, 1)

            def evacuate_mask(i):
                act.wait_ge(mask_turned, i + 1)
                if i >= 2:
                    act.wait_ge(agg, i - 1)
                r = rows(i)
                for b, first, count in ((mask_banks[0], 0, 8), (mask_banks[1], 8, TILES - 8)):
                    src = b[:].bitcast(BF16).rearrange("p (j c) -> p j c", c=P)[:, 0:count, 0:r]
                    nc.scalar.activation(maskT[:, i % 2, first:first + count, 0:r], src, ACT.Copy)\
                      .then_inc(maskT_made, 1)

            for t in range(2, TILES + 2):
                if t < TILES:
                    high_tokens1(t)
                if t == 4:
                    deviations(2)
                u = t - 2
                r = rows(u)
                act.wait_ge(proj, u + 1)
                nc.scalar.activation(y_hi[0:r, u, 0:D], proj_bank[u % 4][0:r, D:2 * D], ACT.Copy)\
                  .then_inc(y_hi_made, 1)
                if t in MASKS_AT:
                    evacuate_mask(MASKS_AT.index(t))
                if 0 <= t - SPLIT0_AT < UNROLL * CHUNK:
                    b, n = divmod(t - SPLIT0_AT, CHUNK)
                    act.wait_ge(v_in[b], 16)
                    split = nc.scalar.activation(v_hi[:, b, n], v_raw[:, b, n], ACT.Copy)
                    if n == CHUNK - 1:
                        split.then_inc(v_hi_made, 1)

            for s in range(TILES + 2):
                if s >= 2:
                    t = s - 2
                    r = rows(t)
                    act.wait_ge(dist2, t + 1)
                    nc.scalar.activation(attn[0:r, t], attn[0:r, t], ACT.Sqrt, scale=float(D)).then_inc(dist, 1)
                if 0 <= s - 1 < TILES:
                    t = s - 1
                    act.wait_ge(turned2, t + 1)
                    nc.scalar.activation(xT_hi[:, :, tok(t)], halves(turn2_bank[t], rows(t)), ACT.Copy)\
                      .then_inc(xT2_hi, 1)
                if s + 2 < TILES:
                    evacuate_mask(s + 2)
                if s < TILES:
                    r = rows(s)
                    act.wait_ge(moments2, s + 1)
                    nc.scalar.activation(std[0:r, s:s + 1], mv[0:r, s, 1:2], ACT.Sqrt, bias=eps[0:r]).then_inc(std2, 1)
                    act.wait_ge(scale2, s + 1)
                    nc.scalar.activation(normed[0:r, s], x_sb[0:r, s], ACT.Identity, scale=rstd[0:r, s:s + 1],
                                         bias=shift[0:r, s:s + 1]).then_inc(norm2, 1)
                if s == 1:
                    act.wait_ge(weights_turned, 4)
                    nc.scalar.activation(woT_hi[:], out_w_bank[:].rearrange("p (k n) -> p k n", k=K), ACT.Copy)\
                      .then_inc(weights_act, 1)
                if s >= 2:
                    t = s - 2
                    r = rows(t)
                    act.wait_ge(inter, t + 1)
                    nc.scalar.activation(attn[0:r, t], attn[0:r, t], ACT.Exp, bias=neg_max[0:r, t:t + 1],
                                         accum_out=total[0:r, t:t + 1]).then_inc(exped, 1)
                    act.wait_ge(total_inv, t + 1)
                    nc.scalar.activation(attn[0:r, t], attn[0:r, t], ACT.Copy, scale=total[0:r, t:t + 1])\
                      .then_inc(attn_made, 1)

            for b in range(UNROLL):
                c = UNROLL + b
                act.wait_ge(v_in[b], 32)
                act.wait_ge(products, (CHUNK0_DONE, TURN_TILES)[b])
                nc.scalar.activation(v_hi[:, b], v_raw[:, b], ACT.Copy).then_inc(v_hi_made, 1)
                if b == 0:
                    act.wait_ge(attn_made, TILES)
                nc.scalar.activation(attn_cur[:, b], attn[:, :, c * CHUNK:(c + 1) * CHUNK], ACT.Copy)\
                  .then_inc(attn_cur_made, 1)

            with nc.Fori(1, TURNS - 1, engines=[mybir.EngineType.Activation]) as i:
                for b in range(UNROLL):
                    act.wait_ge(v_in[b], i * 16 + 32)
                    act.wait_ge(products, i * TURN_TILES + (b + 1) * TILES)
                    nc.scalar.activation(v_hi[:, b], v_raw[:, b], ACT.Copy).then_inc(v_hi_made, 1)
                    act.wait_ge(slot_free, i * TURN_TILES + (b + 1) * TILES)
                    nc.scalar.activation(attn_cur[:, b],
                                         attn[:, :, bass.ds(i * (UNROLL * CHUNK) + (UNROLL + b) * CHUNK, CHUNK)],
                                         ACT.Copy).then_inc(attn_cur_made, 1)

            for t in range(TILES):
                r = rows(t)
                act.wait_ge(o_turned, t + 1)
                if t >= 2:
                    act.wait_ge(o_mult, t - 1)
                nc.scalar.activation(oT_hi[:, t % 2, :, 0:r], halves(o_banks[t][0], r), ACT.Copy)\
                  .then_inc(oT_hi_made, 1)

        @block.vector
        def _(dve):
            steps = [0]

            def then(ins):
                steps[0] += 1
                ins.then_inc(dve_step, 1)
                dve.wait_ge(dve_step, steps[0])

            def moments(g):
                for t in range(TILES)[groups[g]]:
                    r = rows(t)
                    last = nc.vector.bn_stats(stats[0:r, t], x_sb[0:r, t])
                then(last)
                for t in range(TILES)[groups[g]]:
                    r = rows(t)
                    nc.vector.bn_aggr(mv[0:r, t], stats[0:r, t]).then_inc(moments1, 1)

            def scaling(g):
                dve.wait_ge(std1, g + 1)
                then(nc.vector.reciprocal(rstd[:, groups[g]], std[:, groups[g]]))
                nc.vector.scalar_tensor_tensor(shift[:, groups[g]], mv[:, groups[g], 0], -1.0, rstd[:, groups[g]],
                                               ALU.mult, ALU.mult).then_inc(scale1, 1)

            dve.wait_ge(b_cols_in, 32)
            dve.wait_ge(consts_made, 3)
            for w in range(2):
                for k in range(K):
                    nc.vector.tensor_scalar(b_rep[:, w, k], ones[:], b_cols[:, w, k:k + 1], None, ALU.mult)\
                      .then_inc(bias_spread, 1)
            dve.wait_ge(x_in[0], 16)
            moments(0)
            scaling(0)
            for w in range(2):
                dve.wait_ge(weights_act, 3 + w)
                nc.vector.tensor_tensor(w12_lo[:, :, w * D:(w + 1) * D],
                                        w12_bank[w][:].rearrange("p (k n) -> p k n", k=K),
                                        w12_hi[:, :, w * D:(w + 1) * D].bitcast(F32), ALU.subtract)\
                  .then_inc(weights_dve, 1)

            def low_tokens1(t):
                dve.wait_ge(xT1_hi, t + 1)
                nc.vector.tensor_tensor(xT_lo[:, :, tok(t)], halves(turn1_bank[t % 2], rows(t)),
                                        xT_hi[:, :, tok(t)].bitcast(F32), ALU.subtract).then_inc(xT1_lo, 1)

            for t in range(2):
                low_tokens1(t)
            dve.wait_ge(x_in[1], 16)
            moments(1)
            dve.wait_ge(weights_mult, 3)
            dve.wait_ge(b_comb_in, 16)
            then(nc.vector.tensor_tensor(bias_bc[:], bias_bank[:, 0:D], b_comb_bc[:], ALU.add))
            dve.wait_ge(weights_act, 6)
            nc.vector.scalar_tensor_tensor(posT_lo[:], pos_bank[:, 0:K * N].rearrange("p (k n) -> p k n", k=K),
                                           -2.0 / D, posT_hi[:].bitcast(F32), ALU.mult, ALU.subtract)\
              .then_inc(weights_dve, 1)
            scaling(1)

            def make_mask(i):
                dve.wait_ge(adj_in[i % ADJ_RING], 16 * (i // ADJ_RING + 1))
                if i >= 2:
                    dve.wait_ge(mask_turned, i - 1)
                r = rows(i)
                nc.vector.tensor_scalar(mask[0:r, i % 2, 0:T], adj_sb[0:r, i % ADJ_RING, :], 0.0, None, ALU.is_gt)\
                  .then_inc(mask_made, 1)

            for t in range(2, TILES + 2):
                if t < TILES:
                    low_tokens1(t)
                if t == 4:
                    scaling(2)
                u = t - 2
                r = rows(u)
                dve.wait_ge(y_hi_made, u + 1)
                nc.vector.tensor_tensor(y_lo[0:r, u], proj_bank[u % 4][0:r, D:2 * D],
                                        y_hi[0:r, u, 0:D].bitcast(F32), ALU.subtract)
                nc.vector.tensor_tensor(skip[0:r, u], proj_bank[u % 4][0:r, 0:D], bias_bc[0:r, :], ALU.add)\
                  .then_inc(y_made, 1)
                if t == 3:
                    dve.wait_ge(x_in[2], 32)
                    moments(2)
                if t in MASKS_MADE_AT:
                    make_mask(MASKS_MADE_AT.index(t))

            def add_products(before, v, slot, scalars, t, clear=False):
                r = rows(t)
                dve.wait_ge(products, before + (v + 1))
                for n in range(CHUNK):
                    if n >= 2:
                        dve.wait_ge(half_added, before * 2 + (2 * v + n - 1))
                    ps = bank[2 * slot + n // 2][0:r, (n % 2) * D:(n % 2 + 1) * D]
                    a = acc[n % 2][0:r, t]
                    if clear and n < 2:
                        ins = nc.vector.tensor_scalar(a, ps, scalars(n), None, ALU.mult)
                    else:
                        ins = nc.vector.scalar_tensor_tensor(a, ps, scalars(n), a, ALU.mult, ALU.add)
                    if n < 2:
                        ins.then_inc(half_added, 1)
                ins.then_inc(slot_free, 1)

            def first_products(step, chunk):
                for v, (s, b, t) in enumerate(first_turn):
                    if (s, b) == (step, chunk):
                        if b == 0:
                            dve.wait_ge(attn_made, t + 1)
                        add_products(0, v, first_slots[v],
                                     lambda n: attn[0:rows(t), t, b * CHUNK + n:b * CHUNK + n + 1], t, clear=(b == 0))

            def invert_total(t):
                if 0 <= t < TILES:
                    r = rows(t)
                    dve.wait_ge(exped, t + 1)
                    nc.vector.reciprocal(total[0:r, t:t + 1], total[0:r, t:t + 1]).then_inc(total_inv, 1)

            dve.wait_ge(rest_in, 16 * REST_LOADS)
            for s in range(STEPS + 1):
                if s >= LAG[1] + 2:
                    invert_total(s - 3)
                if 0 <= s - 2 < TILES:
                    t = s - 2
                    r = rows(t)
                    dve.wait_ge(z_norm_made, t + 1)
                    dve.wait_ge(cross, t + 1)
                    then(nc.vector.scalar_tensor_tensor(attn[0:r, t], turn2_bank[t][0:r, CROSS:CROSS + N],
                                                        z_norm[0:r, t:t + 1], pos_norm[0:r, :], ALU.add, ALU.add))
                    nc.vector.tensor_scalar(attn[0:r, t], attn[0:r, t], 0.0, None, ALU.max).then_inc(dist2, 1)
                if s < LAG[1] + 2:
                    invert_total(s - 3)
                first_products(s - 1, 0)
                if s < TILES:
                    r = rows(s)
                    dve.wait_ge(agg, s + 1)
                    then(nc.vector.tensor_scalar(rdeg[0:r, s, 0:1], agg_bank[0:r, D:D + 1], 1.0, None, ALU.max))
                    then(nc.vector.reciprocal(rdeg[0:r, s, 1:2], rdeg[0:r, s, 0:1]))
                    nc.vector.scalar_tensor_tensor(skip[0:r, s], agg_bank[0:r, 0:D], rdeg[0:r, s, 1:2],
                                                   skip[0:r, s], ALU.mult, ALU.add).then_inc(agg_read, 1)
                    dve.wait_ge(agg_read, s + 1)
                    then(nc.vector.scalar_tensor_tensor(x_sb[0:r, s], skip[0:r, s], 0.0, x_sb[0:r, s],
                                                        ALU.max, ALU.add))
                if 0 <= s - 1 < TILES:
                    t = s - 1
                    dve.wait_ge(xT2_hi, t + 1)
                    nc.vector.tensor_tensor(xT_lo[:, :, tok(t)], halves(turn2_bank[t], rows(t)),
                                            xT_hi[:, :, tok(t)].bitcast(F32), ALU.subtract).then_inc(xT2_lo, 1)
                if s < TILES:
                    r = rows(s)
                    then(nc.vector.bn_stats(stats[0:r, s], x_sb[0:r, s]))
                    nc.vector.bn_aggr(mv[0:r, s], stats[0:r, s]).then_inc(moments2, 1)
                    dve.wait_ge(std2, s + 1)
                    then(nc.vector.reciprocal(rstd[0:r, s:s + 1], std[0:r, s:s + 1]))
                    nc.vector.scalar_tensor_tensor(shift[0:r, s:s + 1], mv[0:r, s, 0:1], -1.0, rstd[0:r, s:s + 1],
                                                   ALU.mult, ALU.mult).then_inc(scale2, 1)
                if s == 0:
                    dve.wait_ge(weights_mult, 4)
                    nc.vector.tensor_copy(pos_norm[:], pos_bank[:, 0:N]).then_inc(weights_dve, 1)
                if s == 2:
                    dve.wait_ge(weights_act, 7)
                    nc.vector.tensor_tensor(woT_lo[:], out_w_bank[:].rearrange("p (k n) -> p k n", k=K),
                                            woT_hi[:].bitcast(F32), ALU.subtract).then_inc(weights_dve, 1)
                if 0 <= s - 2 < TILES:
                    t = s - 2
                    r = rows(t)
                    dve.wait_ge(dist, t + 1)
                    then(nc.vector.tensor_scalar(attn[0:r, t], attn[0:r, t], SOFTEN, None, ALU.add))
                    then(nc.vector.reciprocal(attn[0:r, t], attn[0:r, t]))
                    then(nc.vector.tensor_tensor_reduce(out=attn[0:r, t], in0=attn[0:r, t], in1=scales_bc[0:r, :],
                                                        scale=1.0, scalar=LOWEST, op0=ALU.mult, op1=ALU.max,
                                                        accum_out=neg_max[0:r, t:t + 1]))
                    nc.vector.tensor_scalar(neg_max[0:r, t:t + 1], neg_max[0:r, t:t + 1], -1.0, None, ALU.mult)\
                      .then_inc(inter, 1)
                if s == STEPS - 2:
                    dve.wait_ge(v_hi_made, UNROLL + 1)
                    nc.vector.tensor_tensor(v_lo[:, 0], v_raw[:, 0], v_hi[:, 0].bitcast(F32), ALU.subtract)\
                      .then_inc(v_made, 1)
                first_products(s, 1)
                if s + 3 < POOL_MASKS:
                    make_mask(s + 3)

            def turn_products(turn, v, slot):
                b, t = divmod(v, TILES)
                if t == 0:
                    dve.wait_ge(attn_cur_made, turn * UNROLL + (b + 1 - UNROLL))
                add_products(turn * TURN_TILES, v, slot, lambda n: attn_cur[0:rows(t), b, t, n:n + 1], t)

            slots, _ = slot_plan(False)
            with nc.Fori(1, LAST_TURN, engines=[mybir.EngineType.DVE], hint_back_edge=True) as i:
                for v in range(TURN_TILES):
                    turn_products(i, v, slots[v])

            def sum_halves(t):
                r = rows(t)
                if t >= 2:
                    dve.wait_ge(o_turned, t - 1)
                dve.wait_ge(slot_free, LAST_TURN * TURN_TILES + (UNROLL - 1) * TILES + t + 1)
                nc.vector.tensor_tensor(o_sum[0:r, t % 2], acc[0][0:r, t], acc[1][0:r, t], ALU.add)\
                  .then_inc(o_summed, 1)

            def low_sums(t):
                r = rows(t)
                dve.wait_ge(oT_hi_made, t + 1)
                nc.vector.tensor_tensor(oT_lo[:, t % 2, :, 0:r], halves(o_banks[t][0], r),
                                        oT_hi[:, t % 2, :, 0:r].bitcast(F32), ALU.subtract).then_inc(oT_made, 1)

            def finish(t):
                r = rows(t)
                dve.wait_ge(o_mult, t + 1)
                dve.wait_ge(residual_made, t + 1)
                if 2 <= t < LAST:
                    dve.wait_ge(stored[t % 2], 16 * (t // 2))
                nc.vector.tensor_tensor(result[t][0:r], o_banks[t][1][0:r, 0:D], x_sb[0:r, t], ALU.add)\
                  .then_inc(result_made, 1)

            for v in range(TURN_TILES):
                turn_products(LAST_TURN, v, last_slots[v])
                t = v - (UNROLL - 1) * TILES
                if t >= 0:
                    sum_halves(t)
                if t >= 1:
                    low_sums(t - 1)
                if t >= 2:
                    finish(t - 2)
            low_sums(LAST)
            finish(LAST - 1)
            finish(LAST)

        @block.tensor
        def _(pe):
            pe.wait_ge(consts_made, 4)
            for _ in range(WARMING):
                nc.tensor.matmul(bank[7][:, 0:P], ones[:], ones[:], start=True, stop=True)
            for w, (src, arrived) in enumerate(((w_self, w_self_in), (w_nb, w_nb_in))):
                pe.wait_ge(arrived, 16)
                for ko in range(K):
                    for kd in range(K):
                        at = (ko * K + kd) * P
                        last = nc.tensor.transpose(wT_bank[w][:, at:at + P], src[:, kd, ko::K], ident[:])
                last.then_inc(weights_turned, 1)
            for w in range(2):
                pe.wait_ge(w_comb_in[w], 16)
                pe.wait_ge(weights_act, w + 1)
                for kd in range(K):
                    for ko in range(K):
                        last = nc.tensor.matmul(w12_bank[w][:, kd * D:(kd + 1) * D], wT[:, w, ko, kd],
                                                w_comb[:, w, ko], start=(ko == 0), stop=(ko == K - 1))
                last.then_inc(weights_mult, 1)

            def turn_tokens(t, dst, signal):
                r = rows(t)
                for k in range(K):
                    last = nc.tensor.transpose(dst[:, k * P:k * P + r], normed[0:r, t, k::K], ident[0:r, 0:r])
                last.then_inc(signal, 1)

            for t in range(2):
                pe.wait_ge(norm1, t + 1)
                turn_tokens(t, turn1_bank[t], turned1)
            pe.wait_ge(bias_spread, 2 * K)
            for w in range(2):
                for k in range(K):
                    last = nc.tensor.matmul(bias_bank[:, 0:D], b_rep[:, w, k], w_comb[:, w, k],
                                            start=(w == k == 0), stop=(w == 1 and k == K - 1))
            last.then_inc(weights_mult, 1)
            pe.wait_ge(pos_in, 16)
            for k in range(K):
                last = nc.tensor.transpose(pos_bank[:, k * N:(k + 1) * N], pos[:, k::K], ident[:])
            last.then_inc(weights_turned, 1)

            def turn_mask(i):
                r = rows(i)
                pe.wait_ge(mask_made, i + 1)
                if i >= 1:
                    pe.wait_ge(maskT_made, 2 * i)
                for j in range(TILES):
                    dst = mask_banks[j // 8][:].bitcast(BF16)
                    at = (j % 8) * P
                    last = nc.tensor.transpose(dst[:, at:at + r], mask[0:r, i % 2, j * P:(j + 1) * P],
                                               ident16[0:r, 0:r])
                last.then_inc(mask_turned, 1)

            for t in range(2, TILES + 2):
                u = t - 2
                r = rows(u)
                if u < 4:
                    pe.wait_ge(weights_dve, (2, 2, 3, 3)[u])
                else:
                    pe.wait_ge(y_made, u - 3)
                pe.wait_ge(xT1_lo, u + 1)
                three_passes(proj_bank[u % 4][0:r, :], lambda k: xT_hi[:, k, tok(u)], lambda k: xT_lo[:, k, tok(u)],
                             lambda k: w12_hi[:, k], lambda k: w12_lo[:, k]).then_inc(proj, 1)
                if t < TILES:
                    pe.wait_ge(norm1, t + 1)
                    pe.wait_ge(xT1_lo, t - 1)
                    turn_tokens(t, turn1_bank[t % 2], turned1)
                if t in MASKS_AT:
                    turn_mask(MASKS_AT.index(t))

            def multiply(slot, b, t):
                r = rows(t)
                pairs = [(bank[2 * slot + h][0:r, :], v_hi[:, b, 2 * h:2 * h + 2], v_lo[:, b, 2 * h:2 * h + 2])
                         for h in range(CHUNK // 2)]
                for k in range(K):
                    hi, lo = xT_hi[:, k, tok(t)], xT_lo[:, k, tok(t)]
                    for ps, vh, vl in pairs:
                        nc.tensor.matmul(ps, hi, vh[:, :, k], start=(k == 0), stop=False)
                    for ps, vh, vl in pairs:
                        nc.tensor.matmul(ps, hi, vl[:, :, k], start=False, stop=False)
                    for ps, vh, vl in pairs:
                        last = nc.tensor.matmul(ps, lo, vh[:, :, k], start=False, stop=(k == K - 1))
                last.then_inc(products, 1)

            def first_products(step, chunk):
                for v, (s, b, t) in enumerate(first_turn):
                    if (s, b) == (step, chunk):
                        if t == 0:
                            pe.wait_ge(v_made, b + 1)
                        if v == 1:
                            pe.wait_ge(weights_dve, 5)
                        if v >= 2:
                            pe.wait_ge(slot_free, v - 1)
                        multiply(first_slots[v], b, t)

            def cross_products(t):
                r = rows(t)
                pe.wait_ge(xT2_lo, t + 1)
                three_passes(turn2_bank[t][0:r, CROSS:CROSS + N], lambda k: xT_hi[:, k, tok(t)],
                             lambda k: xT_lo[:, k, tok(t)], lambda k: posT_hi[:, k], lambda k: posT_lo[:, k])\
                    .then_inc(cross, 1)

            for s in range(STEPS):
                if s < TILES:
                    r = rows(s)
                    pe.wait_ge(maskT_made, 2 * (s + 1))
                    if s == 0:
                        pe.wait_ge(xT1_lo, TILES)
                    else:
                        pe.wait_ge(agg_read, s)
                    for j in range(TILES):
                        c = rows(j)
                        if s == 0:
                            pe.wait_ge(y_made, j + 1)
                        nc.tensor.matmul(agg_bank[0:r, 0:D + 2], maskT[0:c, s % 2, j, 0:r], y_hi[0:c, j],
                                         start=(j == 0), stop=False)
                        last = nc.tensor.matmul(agg_bank[0:r, 0:D], maskT[0:c, s % 2, j, 0:r], y_lo[0:c, j],
                                                start=False, stop=(j == LAST))
                    last.then_inc(agg, 1)
                if 0 <= s - 1 < LAST:
                    t = s - 1
                    pe.wait_ge(norm2, t + 1)
                    if t >= 1:
                        pe.wait_ge(dist2, t)
                    turn_tokens(t, turn2_bank[t], turned2)
                if s + 2 < TILES:
                    turn_mask(s + 2)
                if s == 0:
                    pe.wait_ge(y_made, TILES)
                    for k in range(K):
                        last = nc.tensor.matmul(pos_bank[:, 0:N], ones[:], posT_sq[:, k],
                                                start=(k == 0), stop=(k == K - 1))
                    last.then_inc(weights_mult, 1)
                if s == 1:
                    pe.wait_ge(rest_in, 16 * REST_LOADS)
                    pe.wait_ge(weights_dve, 4)
                    for k in range(K):
                        for b in range(K):
                            at = (k * K + b) * P
                            last = nc.tensor.transpose(out_w_bank[:, at:at + P], w_out[:, b, k::K], ident[:])
                    last.then_inc(weights_turned, 1)
                first_products(s, 1)
                if s == TILES:
                    cross_products(LAST)
                first_products(s, 0)
                if s == LAST:
                    pe.wait_ge(norm2, TILES)
                    pe.wait_ge(agg_read, TILES)
                    turn_tokens(LAST, turn2_bank[LAST], turned2)
                if 0 <= s - 1 < LAST:
                    cross_products(s - 1)

            def turn_products(turn, v, slot, before):
                b, t = divmod(v, TILES)
                if t == 0:
                    pe.wait_ge(v_made, turn * UNROLL + (b + 1))
                pe.wait_ge(slot_free, turn * TURN_TILES + (before + 1))
                multiply(slot, b, t)

            pe.wait_ge(dist2, TILES)
            slots, before = slot_plan(False)
            with nc.Fori(1, LAST_TURN, engines=[mybir.EngineType.PE], hint_back_edge=True) as i:
                for v in range(TURN_TILES):
                    turn_products(i, v, slots[v], before[v])

            def turn_sums(t):
                r = rows(t)
                pe.wait_ge(o_summed, t + 1)
                if t == 0:
                    last_use = max(v for v, slot in enumerate(last_slots) if slot == SLOTS - 1)
                    pe.wait_ge(slot_free, LAST_TURN * TURN_TILES + last_use + 1)
                elif t < LAST:
                    pe.wait_ge(oT_made, t)
                for k in range(K):
                    last = nc.tensor.transpose(o_banks[t][0][:, k * P:k * P + r], o_sum[0:r, t % 2, k::K],
                                               ident[0:r, 0:r])
                last.then_inc(o_turned, 1)

            def project_out(t):
                r = rows(t)
                pe.wait_ge(oT_made, t + 1)
                if 1 <= t < LAST:
                    pe.wait_ge(result_made, t)
                three_passes(o_banks[t][1][0:r, 0:D], lambda k: oT_hi[:, t % 2, k, 0:r],
                             lambda k: oT_lo[:, t % 2, k, 0:r], lambda k: woT_hi[:, k], lambda k: woT_lo[:, k])\
                    .then_inc(o_mult, 1)

            for v in range(TURN_TILES):
                turn_products(LAST_TURN, v, last_slots[v], last_before[v])
                t = v - (UNROLL - 1) * TILES
                if t >= 1:
                    turn_sums(t - 1)
                if t >= 2:
                    project_out(t - 2)
            turn_sums(LAST)
            project_out(LAST - 1)
            project_out(LAST)


_INS = ['x', 'adj', 'L0_gnn_W_self', 'L0_gnn_b_self', 'L0_gnn_W_nb', 'L0_gnn_b_nb', 'L0_gnn_W_comb', 'L0_gnn_b_comb',
        'L0_ffn_positions', 'L0_ffn_scales', 'L0_ffn_value_weight', 'L0_ffn_out_W', 'L0_ffn_out_b']


def kernel(**inputs):
    import numpy as _np
    import concourse.bacc as _bacc
    from concourse import mybir as _mybir
    from concourse.bass_utils import run_bass_kernel_spmd as _run

    nc = _bacc.Bacc("TRN2", target_bir_lowering=False, num_devices=1)
    arrays, args = {}, []
    for name in _INS:
        a = _np.ascontiguousarray(inputs[name])
        arrays[f"in_{name}_dram"] = a
        args.append(nc.dram_tensor(f"in_{name}_dram", a.shape, _mybir.dt.from_np(a.dtype), kind="ExternalInput").ap())
    shape = tuple(inputs['x'].shape)
    args.append(nc.dram_tensor("out_0_dram", shape, _mybir.dt.float32, kind="ExternalOutput").ap())
    gnn_ffn(nc, *args)
    r = _run(nc, [arrays], core_ids=[0])
    return r.results[0]["out_0_dram"]
```
